# Optimizing a Trainium2 kernel written in Bass

```python
import numpy as np
import jax
import jax.numpy as jnp

def _softmax(x, axis=-1):
    return jax.nn.softmax(x, axis=axis)

def _gelu(x):
    return jax.nn.gelu(x, approximate=True)

def _silu(x):
    return jax.nn.silu(x)

def _sigmoid(x):
    return jax.nn.sigmoid(x)

def _layernorm(x, axis=-1, eps=1e-05):
    m = jnp.mean(x, axis=axis, keepdims=True)
    v = jnp.var(x, axis=axis, keepdims=True)
    return (x - m) / jnp.sqrt(v + eps)

def _scatter_add(tgt, idx, src, axis=0):
    return tgt.at[idx].add(src)

def _segment_sum(src, seg, n):
    return jax.ops.segment_sum(src, seg, n)
kernel_name = 'mk_dlrm_tower_d1_rec_r8_8c47dd'

def setup_inputs(seed: int=0):
    np.random.seed(seed)
    _w = jnp.asarray

    def _rec_inputs():
        import jax
        import jax.numpy as jnp
        _tk = jax.random.key(seed)
        dense_ctx = jax.random.normal(jax.random.fold_in(_tk, 190), (2048, 16), jnp.float32)
        ids = jnp.stack([jax.random.randint(jax.random.fold_in(_tk, 200 + f), (2048,), 0, v, jnp.int32) for f, v in enumerate([1000, 1000, 1250, 1250, 1000, 1000, 1000, 1000, 1000, 12500, 12500, 1250, 1250, 1250, 1250, 1000, 12500, 1250, 12500, 1000, 1000, 1250, 1000, 1250, 1000, 12500, 12500, 1000, 1250, 12500, 12500, 1000])], axis=1)
        tbl_0 = 0.05 * jax.random.normal(jax.random.fold_in(_tk, 500 + 0), (1000, 256), jnp.float32)
        tbl_1 = 0.05 * jax.random.normal(jax.random.fold_in(_tk, 500 + 1), (1000, 256), jnp.float32)
        tbl_2 = 0.05 * jax.random.normal(jax.random.fold_in(_tk, 500 + 2), (1250, 256), jnp.float32)
        tbl_3 = 0.05 * jax.random.normal(jax.random.fold_in(_tk, 500 + 3), (1250, 256), jnp.float32)
        tbl_4 = 0.05 * jax.random.normal(jax.random.fold_in(_tk, 500 + 4), (1000, 256), jnp.float32)
        tbl_5 = 0.05 * jax.random.normal(jax.random.fold_in(_tk, 500 + 5), (1000, 256), jnp.float32)
        tbl_6 = 0.05 * jax.random.normal(jax.random.fold_in(_tk, 500 + 6), (1000, 256), jnp.float32)
        tbl_7 = 0.05 * jax.random.normal(jax.random.fold_in(_tk, 500 + 7), (1000, 256), jnp.float32)
        tbl_8 = 0.05 * jax.random.normal(jax.random.fold_in(_tk, 500 + 8), (1000, 256), jnp.float32)
        tbl_9 = 0.05 * jax.random.normal(jax.random.fold_in(_tk, 500 + 9), (12500, 256), jnp.float32)
        tbl_10 = 0.05 * jax.random.normal(jax.random.fold_in(_tk, 500 + 10), (12500, 256), jnp.float32)
        tbl_11 = 0.05 * jax.random.normal(jax.random.fold_in(_tk, 500 + 11), (1250, 256), jnp.float32)
        tbl_12 = 0.05 * jax.random.normal(jax.random.fold_in(_tk, 500 + 12), (1250, 256), jnp.float32)
        tbl_13 = 0.05 * jax.random.normal(jax.random.fold_in(_tk, 500 + 13), (1250, 256), jnp.float32)
        tbl_14 = 0.05 * jax.random.normal(jax.random.fold_in(_tk, 500 + 14), (1250, 256), jnp.float32)
        tbl_15 = 0.05 * jax.random.normal(jax.random.fold_in(_tk, 500 + 15), (1000, 256), jnp.float32)
        tbl_16 = 0.05 * jax.random.normal(jax.random.fold_in(_tk, 500 + 16), (12500, 256), jnp.float32)
        tbl_17 = 0.05 * jax.random.normal(jax.random.fold_in(_tk, 500 + 17), (1250, 256), jnp.float32)
        tbl_18 = 0.05 * jax.random.normal(jax.random.fold_in(_tk, 500 + 18), (12500, 256), jnp.float32)
        tbl_19 = 0.05 * jax.random.normal(jax.random.fold_in(_tk, 500 + 19), (1000, 256), jnp.float32)
        tbl_20 = 0.05 * jax.random.normal(jax.random.fold_in(_tk, 500 + 20), (1000, 256), jnp.float32)
        tbl_21 = 0.05 * jax.random.normal(jax.random.fold_in(_tk, 500 + 21), (1250, 256), jnp.float32)
        tbl_22 = 0.05 * jax.random.normal(jax.random.fold_in(_tk, 500 + 22), (1000, 256), jnp.float32)
        tbl_23 = 0.05 * jax.random.normal(jax.random.fold_in(_tk, 500 + 23), (1250, 256), jnp.float32)
        tbl_24 = 0.05 * jax.random.normal(jax.random.fold_in(_tk, 500 + 24), (1000, 256), jnp.float32)
        tbl_25 = 0.05 * jax.random.normal(jax.random.fold_in(_tk, 500 + 25), (12500, 256), jnp.float32)
        tbl_26 = 0.05 * jax.random.normal(jax.random.fold_in(_tk, 500 + 26), (12500, 256), jnp.float32)
        tbl_27 = 0.05 * jax.random.normal(jax.random.fold_in(_tk, 500 + 27), (1000, 256), jnp.float32)
        tbl_28 = 0.05 * jax.random.normal(jax.random.fold_in(_tk, 500 + 28), (1250, 256), jnp.float32)
        tbl_29 = 0.05 * jax.random.normal(jax.random.fold_in(_tk, 500 + 29), (12500, 256), jnp.float32)
        tbl_30 = 0.05 * jax.random.normal(jax.random.fold_in(_tk, 500 + 30), (12500, 256), jnp.float32)
        tbl_31 = 0.05 * jax.random.normal(jax.random.fold_in(_tk, 500 + 31), (1000, 256), jnp.float32)
        _rk = jax.random.fold_in(_tk, 7)
        W_top1 = 0.0441942 * jax.random.normal(jax.random.fold_in(_tk, 801), (512, 512), jnp.float32)
        W_top2 = 0.0441942 * jax.random.normal(jax.random.fold_in(_tk, 802), (512, 256), jnp.float32)
        W_top3 = 0.0625 * jax.random.normal(jax.random.fold_in(_tk, 803), (256, 1), jnp.float32)
        b_top1 = jnp.zeros((512,), jnp.float32)
        b_top2 = jnp.zeros((256,), jnp.float32)
        return (dense_ctx, ids, tbl_0, tbl_1, tbl_2, tbl_3, tbl_4, tbl_5, tbl_6, tbl_7, tbl_8, tbl_9, tbl_10, tbl_11, tbl_12, tbl_13, tbl_14, tbl_15, tbl_16, tbl_17, tbl_18, tbl_19, tbl_20, tbl_21, tbl_22, tbl_23, tbl_24, tbl_25, tbl_26, tbl_27, tbl_28, tbl_29, tbl_30, tbl_31, W_top1, b_top1, W_top2, b_top2, W_top3)
    dense_ctx, ids, tbl_0, tbl_1, tbl_2, tbl_3, tbl_4, tbl_5, tbl_6, tbl_7, tbl_8, tbl_9, tbl_10, tbl_11, tbl_12, tbl_13, tbl_14, tbl_15, tbl_16, tbl_17, tbl_18, tbl_19, tbl_20, tbl_21, tbl_22, tbl_23, tbl_24, tbl_25, tbl_26, tbl_27, tbl_28, tbl_29, tbl_30, tbl_31, W_top1, b_top1, W_top2, b_top2, W_top3 = _rec_inputs()

    def _L0_rec_setup():
        import jax, jax.numpy as jnp
        import numpy as np
        B, N, D = (1024, 32, 256)
        key = jax.random.key(seed)
        x = jax.random.normal(key, (B, N, D), dtype=jnp.float32)
        return {'x': x}
    _L0_rec_all = _L0_rec_setup()
    _L0_rec_in = {k: v for k, v in _L0_rec_all.items() if k in ()}
    del _L0_rec_all
    return {'dense_ctx': dense_ctx, 'ids': ids, 'tbl_0': tbl_0, 'tbl_1': tbl_1, 'tbl_2': tbl_2, 'tbl_3': tbl_3, 'tbl_4': tbl_4, 'tbl_5': tbl_5, 'tbl_6': tbl_6, 'tbl_7': tbl_7, 'tbl_8': tbl_8, 'tbl_9': tbl_9, 'tbl_10': tbl_10, 'tbl_11': tbl_11, 'tbl_12': tbl_12, 'tbl_13': tbl_13, 'tbl_14': tbl_14, 'tbl_15': tbl_15, 'tbl_16': tbl_16, 'tbl_17': tbl_17, 'tbl_18': tbl_18, 'tbl_19': tbl_19, 'tbl_20': tbl_20, 'tbl_21': tbl_21, 'tbl_22': tbl_22, 'tbl_23': tbl_23, 'tbl_24': tbl_24, 'tbl_25': tbl_25, 'tbl_26': tbl_26, 'tbl_27': tbl_27, 'tbl_28': tbl_28, 'tbl_29': tbl_29, 'tbl_30': tbl_30, 'tbl_31': tbl_31, 'W_top1': W_top1, 'b_top1': b_top1, 'W_top2': W_top2, 'b_top2': b_top2, 'W_top3': W_top3}

def reference(dense_ctx, ids, tbl_0, tbl_1, tbl_2, tbl_3, tbl_4, tbl_5, tbl_6, tbl_7, tbl_8, tbl_9, tbl_10, tbl_11, tbl_12, tbl_13, tbl_14, tbl_15, tbl_16, tbl_17, tbl_18, tbl_19, tbl_20, tbl_21, tbl_22, tbl_23, tbl_24, tbl_25, tbl_26, tbl_27, tbl_28, tbl_29, tbl_30, tbl_31, W_top1, b_top1, W_top2, b_top2, W_top3):
    import jax
    import jax.numpy as jnp

    def _L0_rec_ref(x):
        import jax, jax.numpy as jnp
        import numpy as np
        B, N, D = (1024, 32, 256)
        'Second-order feature interaction (DLRM dot interaction).\n\n            Computes dot(x_i, x_j) for all field pairs i < j (self_interaction=False),\n            flattened in row-major upper-triangular order -> [B, N*(N-1)/2].\n            Matches tf.boolean_mask(dot_products, strictly_upper_mask) ordering.\n            '
        b, n, d = x.shape
        iu, ju = jnp.triu_indices(n, k=1)
        dots = jnp.einsum('bnd,bmd->bnm', x, x)
        return dots[:, iu, ju]
    e = jnp.stack([tbl_0[ids[:, 0]], tbl_1[ids[:, 1]], tbl_2[ids[:, 2]], tbl_3[ids[:, 3]], tbl_4[ids[:, 4]], tbl_5[ids[:, 5]], tbl_6[ids[:, 6]], tbl_7[ids[:, 7]], tbl_8[ids[:, 8]], tbl_9[ids[:, 9]], tbl_10[ids[:, 10]], tbl_11[ids[:, 11]], tbl_12[ids[:, 12]], tbl_13[ids[:, 13]], tbl_14[ids[:, 14]], tbl_15[ids[:, 15]], tbl_16[ids[:, 16]], tbl_17[ids[:, 17]], tbl_18[ids[:, 18]], tbl_19[ids[:, 19]], tbl_20[ids[:, 20]], tbl_21[ids[:, 21]], tbl_22[ids[:, 22]], tbl_23[ids[:, 23]], tbl_24[ids[:, 24]], tbl_25[ids[:, 25]], tbl_26[ids[:, 26]], tbl_27[ids[:, 27]], tbl_28[ids[:, 28]], tbl_29[ids[:, 29]], tbl_30[ids[:, 30]], tbl_31[ids[:, 31]]], axis=1)
    z = _L0_rec_ref(e)
    z = z.reshape(z.shape[0], -1)
    h = jnp.concatenate([z, dense_ctx], axis=1)
    h = jnp.maximum(h @ W_top1 + b_top1, 0.0)
    h = jnp.maximum(h @ W_top2 + b_top2, 0.0)
    y = h @ W_top3
    return y

_drawn_inputs = setup_inputs


def setup_inputs(seed=0):
    import zlib

    import numpy as np

    out = dict(_drawn_inputs(seed))
    spreads = {'b_top1': (0.0, 0.1), 'b_top2': (0.0, 0.1)}
    factors = {}
    for name, (base, spread) in spreads.items():
        noise = np.random.default_rng([zlib.crc32(name.encode()), seed]).standard_normal(out[name].shape)
        drawn = base * np.exp(spread * noise) if base else spread * noise
        out[name] = jnp.asarray(drawn.astype(out[name].dtype))
    for name, factor in factors.items():
        out[name] = (out[name] * factor).astype(out[name].dtype)
    return out
```

```python
import concourse.bass as bass
from concourse import mybir
from contextlib import ExitStack

P = 128
D_HALVES = 2
QUAD = 4
CHUNK = 8
TILES_PER_PAIR = 2
DMA = 16


def build(nc, dense_ctx, ids, tables, w1, b1, w2, b2, w3, y):
    f32, i32, u32 = mybir.dt.float32, mybir.dt.int32, mybir.dt.uint32
    ALU, ACT = mybir.AluOpType, mybir.ActivationFunctionType

    batch, fields = ids.shape
    width = tables[0].shape[1]
    ctx_width = dense_ctx.shape[1]
    h1, h2 = w1.shape[1], w2.shape[1]
    pairs_of_fields = fields * (fields - 1) // 2
    features = pairs_of_fields + ctx_width
    tiles = batch // P
    pairs = tiles // TILES_PER_PAIR
    chunks = fields // CHUNK
    quads = CHUNK // QUAD
    groups = P // QUAD
    chunk_groups = groups // chunks
    pair_groups = groups * TILES_PER_PAIR
    cols = TILES_PER_PAIR * P
    k1, m1, m2 = features // P, h1 // P, h2 // P
    tri_fills = fields // QUAD
    assert width == D_HALVES * P and features == k1 * P and chunks == 4 and m1 == 4 and m2 == 2

    TRI, PACK, LAYER1, LAYER2, LAYER3 = 4, 5, 6, 7, 8
    FILLS = (8, 7)

    def first_of_row(i):
        return i * (fields - 1) - i * (i - 1) // 2

    with ExitStack() as ctx:
        def sbuf(name, shape, dt=f32):
            return ctx.enter_context(nc.sbuf_tensor(name, shape, dt))

        def psum(name, shape):
            return ctx.enter_context(nc.psum_tensor(name, shape, f32))

        def sem(name):
            return ctx.enter_context(nc.semaphore(name))

        ids_sb = sbuf("ids_sb", [P, TILES_PER_PAIR, fields], i32)
        rows = [sbuf(f"rows{c}", [P, CHUNK, width]) for c in range(chunks)]
        emb_t = [sbuf(f"emb_t{u}", [P, D_HALVES, P, fields]) for u in range(TILES_PER_PAIR)]
        dots = sbuf("dots", [P, fields, pair_groups])
        packed = sbuf("packed", [pair_groups, QUAD, features])
        feat_t = sbuf("feat_t", [P, k1, cols])
        hid1_t = sbuf("hid1_t", [P, m1, cols])
        hid2_t = sbuf("hid2_t", [P, m2, cols])
        y_row = sbuf("y_row", [1, cols])
        w1_sb = sbuf("w1_sb", [P, k1, h1])
        w2_sb = sbuf("w2_sb", [P, m1, h2])
        w3_sb = sbuf("w3_sb", [P, m2])
        b1_sb = sbuf("b1_sb", [P, m1])
        b2_sb = sbuf("b2_sb", [P, m2])
        ident = sbuf("ident", [P, P])

        tr_ps = [psum(f"tr_ps{h}", [P, QUAD, P]) for h in range(D_HALVES)]
        gram_ps = [psum(f"gram_ps{k}", [P, chunk_groups, P]) for k in range(2)]
        mlp_ps = [psum(f"mlp_ps{k}", [P, 512]) for k in range(2)]

        ids_loaded = [sem(f"ids_loaded{u}") for u in range(TILES_PER_PAIR)]
        rows_loaded = [sem(f"rows_loaded{c}") for c in range(chunks)]
        weights_loaded = sem("weights_loaded")
        ctx_loaded = sem("ctx_loaded")
        ident_filled = sem("ident_filled")
        ident_ready = sem("ident_ready")
        transposed = [sem(f"transposed{h}") for h in range(D_HALVES)]
        emb_copied = [sem(f"emb_copied{h}") for h in range(D_HALVES)]
        gram_done = [sem(f"gram_done{k}") for k in range(2)]
        dots_copied = [sem(f"dots_copied{k}") for k in range(2)]
        mlp_done = [sem(f"mlp_done{k}") for k in range(2)]
        mlp_copied = [sem(f"mlp_copied{k}") for k in range(2)]
        y_stored = sem("y_stored")
        pool_let_go = sem("pool_let_go")
        pe_let_go = sem("pe_let_go")

        def wait(eng, s, value):
            if not (isinstance(value, int) and value <= 0):
                eng.wait_ge(s, value)

        block = ctx.enter_context(nc.Block())

        @block.sync
        def _(sp):
            def load_ids(p, u):
                sp.dma_start(ids_sb[:, u, :], ids[bass.ds(p * cols + u * P, P), :]).then_inc(ids_loaded[u], DMA)

            def load_ctx(p):
                if not isinstance(p, int):
                    sp.wait_ge(mlp_done[1], (p - 1) * FILLS[1] + PACK)
                sp.dma_start(packed[:, :, pairs_of_fields:],
                             dense_ctx[bass.ds(p * cols, cols), :].rearrange("(g b) c -> g b c", b=QUAD)
                             ).then_inc(ctx_loaded, DMA)

            def store_y(p):
                sp.wait_ge(mlp_copied[0], p * FILLS[0] + LAYER3)
                sp.dma_start(y[bass.ds(p * cols, cols), :].rearrange("n o -> o n"), y_row[:]
                             ).then_inc(y_stored, DMA)

            load_ids(0, 0)
            load_ids(0, 1)
            sp.dma_start(w1_sb[:], w1.rearrange("(k p) n -> p k n", p=P)).then_inc(weights_loaded, DMA)
            sp.dma_start(w2_sb[:], w2.rearrange("(k p) n -> p k n", p=P)).then_inc(weights_loaded, DMA)
            with nc.allow_non_contiguous_dma(reason="columns of a few hundred words, once"):
                sp.dma_start(w3_sb[:], w3.rearrange("(k p) o -> p (k o)", p=P)).then_inc(weights_loaded, DMA)
                sp.dma_start(b1_sb[:], b1.rearrange("(k p) -> p k", p=P)).then_inc(weights_loaded, DMA)
                sp.dma_start(b2_sb[:], b2.rearrange("(k p) -> p k", p=P)).then_inc(weights_loaded, DMA)
            load_ctx(0)
            with sp.Fori(1, pairs) as p:
                for u in range(TILES_PER_PAIR):
                    sp.wait_ge(transposed[1], ((p - 1) * TILES_PER_PAIR + u + 1) * chunks * quads)
                    load_ids(p, u)
                load_ctx(p)
                store_y(p - 1)
            store_y(pairs - 1)
            sp.wait_ge(y_stored, DMA * pairs)

        @block.gpsimd
        def _(pool):
            def gather_tile(p, u, c):
                t = p * TILES_PER_PAIR + u
                if c == 0:
                    pool.wait_ge(ids_loaded[u], (p + 1) * DMA)
                wait(pool, transposed[1], ((t - 1) * chunks + c + 1) * quads
                     if not isinstance(t, int) or t > 0 else 0)
                pool.sem_inc(pool_let_go, 1)
                for j in range(CHUNK):
                    f = c * CHUNK + j
                    pool.indirect_dma_start(
                        out=rows[c][:, j, :], out_offset=None, in_=tables[f],
                        in_offset=bass.IndirectOffsetOnAxis(ap=ids_sb[:, u, f:f + 1].bitcast(u32), axis=0),
                    ).then_inc(rows_loaded[c], DMA)

            gather_tile(0, 0, 0)
            nc.gpsimd.memset(ident[:], 1.0).then_inc(ident_filled, 1)
            pool.wait_ge(ident_filled, 1)
            nc.gpsimd.affine_select(out=ident[:], in_=ident[:], compare_op=ALU.is_equal, fill=0.0, base=0,
                                    pattern=[[-1, P]], channel_multiplier=1).then_inc(ident_ready, 1)
            for c in range(1, chunks):
                gather_tile(0, 0, c)
            for c in range(chunks):
                gather_tile(0, 1, c)
            with pool.Fori(1, pairs) as p:
                for u in range(TILES_PER_PAIR):
                    for c in range(chunks):
                        gather_tile(p, u, c)

        @block.tensor
        def _(pe):
            def transpose_quad(p, u, c, q):
                n = ((p * TILES_PER_PAIR + u) * chunks + c) * quads + q
                if q == 0:
                    pe.wait_ge(rows_loaded[c], (p * TILES_PER_PAIR + u + 1) * CHUNK * DMA)
                for h in range(D_HALVES):
                    wait(pe, emb_copied[h], n)
                    for j in range(QUAD):
                        last = nc.tensor.transpose(tr_ps[h][:, j, :], rows[c][:, q * QUAD + j, h * P:(h + 1) * P],
                                                   ident[:])
                    last.then_inc(transposed[h], 1)

            def gram(p, u, c, part):
                t = p * TILES_PER_PAIR + u
                if part == 0:
                    if c == 0:
                        for h in range(D_HALVES):
                            pe.wait_ge(emb_copied[h], (t + 1) * chunks * quads)
                    wait(pe, dots_copied[c % 2], t * 2 + c // 2)
                half = chunk_groups // 2
                for g in range(part * half, (part + 1) * half):
                    s = (c * chunk_groups + g) * QUAD
                    for h in range(D_HALVES):
                        four = emb_t[u][:, h, s:s + QUAD, :].rearrange("p s f -> p (s f)")
                        last = nc.tensor.matmul(gram_ps[c % 2][:, g, :], four, four,
                                                start=(h == 0), stop=(h == D_HALVES - 1))
                if part == 1:
                    last.then_inc(gram_done[c % 2], 1)

            def all_copied(p, fills):
                for k in range(2):
                    pe.wait_ge(mlp_copied[k], p * FILLS[k] + min(fills, FILLS[k]))

            def tri(p, fill):
                k = fill % 2
                if fill == 0:
                    for j in range(2):
                        pe.wait_ge(dots_copied[j], (p + 1) * TILES_PER_PAIR * 2)
                wait(pe, mlp_copied[k], p * FILLS[k] + fill // 2)
                pe.sem_inc(pe_let_go, 1)
                for j in range(QUAD):
                    i = fill * QUAD + j
                    if i < fields - 1:
                        last = nc.tensor.transpose(mlp_ps[k][0:pair_groups, j * P:(j + 1) * P], dots[:, i, :], ident[:])
                last.then_inc(mlp_done[k], 1)

            def pack(p):
                all_copied(p, TRI)
                pe.wait_ge(ctx_loaded, (p + 1) * DMA)
                pe.sem_inc(pe_let_go, 1)
                for k in range(2):
                    for j in range(k1 // 2):
                        for b in range(QUAD):
                            f = (k * k1 // 2 + j) * P
                            at = j * cols + b * pair_groups
                            last = nc.tensor.transpose(mlp_ps[k][:, at:at + pair_groups], packed[:, b, f:f + P],
                                                       ident[0:pair_groups, 0:pair_groups])
                    last.then_inc(mlp_done[k], 1)

            def layer1(p):
                all_copied(p, PACK)
                for m in range(m1):
                    k = m * 2 // m1
                    at = (m % (m1 // 2)) * cols
                    for i in range(k1):
                        last = nc.tensor.matmul(mlp_ps[k][:, at:at + cols], w1_sb[:, i, m * P:(m + 1) * P],
                                                feat_t[:, i, :], start=(i == 0), stop=(i == k1 - 1))
                    if m % (m1 // 2) == m1 // 2 - 1:
                        last.then_inc(mlp_done[k], 1)

            def layer2(p):
                all_copied(p, LAYER1)
                for m in range(m2):
                    for i in range(m1):
                        last = nc.tensor.matmul(mlp_ps[m][:, 0:cols], w2_sb[:, i, m * P:(m + 1) * P],
                                                hid1_t[:, i, :], start=(i == 0), stop=(i == m1 - 1))
                    last.then_inc(mlp_done[m], 1)

            def layer3(p):
                all_copied(p, LAYER2)
                for i in range(m2):
                    last = nc.tensor.matmul(mlp_ps[0][0:1, 0:cols], w3_sb[:, i:i + 1], hid2_t[:, i, :],
                                            start=(i == 0), stop=(i == m2 - 1))
                last.then_inc(mlp_done[0], 1)

            def step(p, u, c, gram_of, layers_of):
                transpose_quad(p, u, c, 0)
                if layers_of is not None and c == 0:
                    for fill in range(tri_fills // 2):
                        tri(layers_of, fill)
                elif gram_of is not None:
                    gram(*gram_of, c, 0)
                transpose_quad(p, u, c, 1)
                if layers_of is not None:
                    if c == 0:
                        for fill in range(tri_fills // 2, tri_fills):
                            tri(layers_of, fill)
                        gram(*gram_of, c, 0)
                    else:
                        (pack, layer1, layer2)[c - 1](layers_of)
                if gram_of is not None:
                    gram(*gram_of, c, 1)
                if layers_of is not None and c == chunks - 1:
                    layer3(layers_of)

            pe.wait_ge(ident_ready, 1)
            for c in range(chunks):
                step(0, 0, c, None, None)
            for c in range(chunks):
                step(0, 1, c, (0, 0), None)
            pe.wait_ge(weights_loaded, 5 * DMA)
            with pe.Fori(1, pairs) as p:
                for c in range(chunks):
                    step(p, 0, c, (p - 1, 1), None)
                for c in range(chunks):
                    step(p, 1, c, (p, 0), p - 1)
            last_pair = pairs - 1
            for c in range(chunks):
                for part in range(2):
                    gram(last_pair, 1, c, part)
            for fill in range(tri_fills):
                tri(last_pair, fill)
            for stage in (pack, layer1, layer2, layer3):
                stage(last_pair)

        def copies(eng, who, copy, bias_relu):
            def emb_copy(p, u, c, q):
                n = ((p * TILES_PER_PAIR + u) * chunks + c) * quads + q
                f = c * CHUNK + q * QUAD
                eng.wait_ge(transposed[who], n + 1)
                copy(emb_t[u][:, who, :, f:f + QUAD].rearrange("p s f -> p f s"), tr_ps[who][:]
                     ).then_inc(emb_copied[who], 1)

            def dots_copy(p, u, c):
                if c % 2 != who:
                    return
                eng.wait_ge(gram_done[who], (p * TILES_PER_PAIR + u) * 2 + c // 2 + 1)
                g = u * groups + c * chunk_groups
                for b in range(QUAD):
                    own = slice(b * fields, (b + 1) * fields)
                    last = copy(dots[own, :, g:g + chunk_groups].rearrange("p j g -> p g j"), gram_ps[who][own, :, own])
                last.then_inc(dots_copied[who], 1)

            def stage_ready(p, fills):
                eng.wait_ge(mlp_done[who], p * FILLS[who] + fills)

            def tri_copy(p, fill):
                if fill % 2 != who:
                    return
                stage_ready(p, fill // 2 + 1)
                for j in range(QUAD):
                    i = fill * QUAD + j
                    if i < fields - 1:
                        n = fields - 1 - i
                        at = first_of_row(i)
                        seen = mlp_ps[who][0:pair_groups, j * P:(j + 1) * P].rearrange("g (b f) -> g b f", b=QUAD)
                        last = copy(packed[:, :, at:at + n], seen[:, :, i + 1:fields])
                last.then_inc(mlp_copied[who], 1)

            def pack_copy(p):
                stage_ready(p, PACK)
                for j in range(k1 // 2):
                    k = who * k1 // 2 + j
                    last = copy(feat_t[:, k, :].rearrange("p (g b) -> p b g", b=QUAD),
                                mlp_ps[who][:, j * cols:(j + 1) * cols].rearrange("p (b g) -> p b g", b=QUAD))
                last.then_inc(mlp_copied[who], 1)

            def layer1_copy(p):
                stage_ready(p, LAYER1)
                for j in range(m1 // 2):
                    m = who * m1 // 2 + j
                    last = bias_relu(hid1_t[:, m, :], mlp_ps[who][:, j * cols:(j + 1) * cols], b1_sb[:, m:m + 1])
                last.then_inc(mlp_copied[who], 1)

            def layer2_copy(p):
                stage_ready(p, LAYER2)
                bias_relu(hid2_t[:, who, :], mlp_ps[who][:, 0:cols], b2_sb[:, who:who + 1]
                          ).then_inc(mlp_copied[who], 1)

            def layer3_copy(p):
                if who == 0:
                    stage_ready(p, LAYER3)
                    wait(eng, y_stored, p * DMA)
                    copy(y_row[:], mlp_ps[0][0:1, 0:cols]).then_inc(mlp_copied[0], 1)

            def step(p, u, c, gram_of, layers_of):
                emb_copy(p, u, c, 0)
                if layers_of is not None and c == 0:
                    for fill in range(tri_fills // 2):
                        tri_copy(layers_of, fill)
                emb_copy(p, u, c, 1)
                if layers_of is not None:
                    if c == 0:
                        for fill in range(tri_fills // 2, tri_fills):
                            tri_copy(layers_of, fill)
                    else:
                        (pack_copy, layer1_copy, layer2_copy)[c - 1](layers_of)
                if gram_of is not None:
                    dots_copy(*gram_of, c)
                if layers_of is not None and c == chunks - 1:
                    layer3_copy(layers_of)

            for c in range(chunks):
                step(0, 0, c, None, None)
            for c in range(chunks):
                step(0, 1, c, (0, 0), None)
            eng.wait_ge(weights_loaded, 5 * DMA)
            with eng.Fori(1, pairs) as p:
                for c in range(chunks):
                    step(p, 0, c, (p - 1, 1), None)
                for c in range(chunks):
                    step(p, 1, c, (p, 0), p - 1)
            last_pair = pairs - 1
            for c in range(chunks):
                dots_copy(last_pair, 1, c)
            for fill in range(tri_fills):
                tri_copy(last_pair, fill)
            for stage in (pack_copy, layer1_copy, layer2_copy, layer3_copy):
                stage(last_pair)

        @block.vector
        def _(dve):
            copies(dve, 0, nc.vector.tensor_copy,
                   lambda out, x, bias: nc.vector.tensor_scalar(out, x, bias, 0.0, ALU.add, ALU.max))

        @block.scalar
        def _(act):
            copies(act, 1, nc.scalar.copy,
                   lambda out, x, bias: nc.scalar.activation(out, x, ACT.Relu, bias=bias))


def kernel(**inputs):
    import numpy as np
    import concourse.bacc as bacc
    from concourse.bass_utils import run_bass_kernel_spmd

    nc = bacc.Bacc("TRN2", target_bir_lowering=False, num_devices=1)
    arrays, aps = {}, {}
    for name, a in inputs.items():
        a = np.ascontiguousarray(a)
        arrays[f"in_{name}"] = a
        aps[name] = nc.dram_tensor(f"in_{name}", a.shape, mybir.dt.from_np(a.dtype), kind="ExternalInput").ap()
    batch, fields = inputs["ids"].shape
    y = nc.dram_tensor("out_y", (batch, 1), mybir.dt.float32, kind="ExternalOutput").ap()
    build(nc, aps["dense_ctx"], aps["ids"], [aps[f"tbl_{f}"] for f in range(fields)],
          aps["W_top1"], aps["b_top1"], aps["W_top2"], aps["b_top2"], aps["W_top3"], y)
    r = run_bass_kernel_spmd(nc, [arrays], core_ids=[0])
    return r.results[0]["out_y"]
```

```python
import concourse.bass as bass
from concourse import mybir
from contextlib import ExitStack

P = 128
D_HALVES = 2
QUAD = 4
CHUNK = 8
BUFFERS = 2
DMA = 16


def build(nc, dense_ctx, ids, tables, w1, b1, w2, b2, w3, y):
    f32, i32, u32 = mybir.dt.float32, mybir.dt.int32, mybir.dt.uint32
    ALU, ACT = mybir.AluOpType, mybir.ActivationFunctionType

    batch, fields = ids.shape
    width = tables[0].shape[1]
    ctx_width = dense_ctx.shape[1]
    h1, h2 = w1.shape[1], w2.shape[1]
    pairs_of_fields = fields * (fields - 1) // 2
    features = pairs_of_fields + ctx_width
    tiles = batch // P
    chunks = fields // CHUNK
    quads = CHUNK // QUAD
    groups = P // QUAD
    bank_groups = 4
    gram_fills = groups // bank_groups
    gram_fills_each = gram_fills // 2
    k1, m1, m2 = features // P, h1 // P, h2 // P
    per_transpose = P // groups
    assert width == D_HALVES * P and features == k1 * P and fields * groups == 2 * 4 * P
    assert chunks == 4 and m1 == 4 and m2 == 2 and tiles % BUFFERS == 0

    TRI, PACK, LAYER1, LAYER2, LAYER3 = 1, 2, 3, 4, 5
    FILLS = (LAYER3, LAYER2)

    def first_of_row(i):
        return i * (fields - 1) - i * (i - 1) // 2

    def tri_place(i):
        block = i // per_transpose
        return block % 2, i % per_transpose * groups, block // 2 * P

    with ExitStack() as ctx:
        def sbuf(name, shape, dt=f32):
            return ctx.enter_context(nc.sbuf_tensor(name, shape, dt))

        def psum(name, shape):
            return ctx.enter_context(nc.psum_tensor(name, shape, f32))

        def sem(name):
            return ctx.enter_context(nc.semaphore(name))

        ids_sb = sbuf("ids_sb", [P, BUFFERS, fields], i32)
        rows = [sbuf(f"rows{c}", [P, CHUNK, width]) for c in range(chunks)]
        emb_t = [sbuf(f"emb_t{u}", [P, D_HALVES, P, fields]) for u in range(BUFFERS)]
        dots = sbuf("dots", [P, fields, groups])
        packed = sbuf("packed", [groups, QUAD, features])
        feat_t = sbuf("feat_t", [P, k1, P])
        hid1_t = sbuf("hid1_t", [P, m1, P])
        hid2_t = sbuf("hid2_t", [P, m2, P])
        y_row = sbuf("y_row", [1, BUFFERS * P])
        w1_sb = sbuf("w1_sb", [P, k1, h1])
        w2_sb = sbuf("w2_sb", [P, m1, h2])
        w3_sb = sbuf("w3_sb", [P, m2])
        b1_sb = sbuf("b1_sb", [P, m1])
        b2_sb = sbuf("b2_sb", [P, m2])
        ident = sbuf("ident", [P, P])

        tr_ps = [[psum(f"tr_ps{h}{q}", [P, QUAD, P]) for q in range(quads)] for h in range(D_HALVES)]
        gram_ps = [psum(f"gram_ps{k}", [P, bank_groups, P]) for k in range(2)]
        mlp_ps = [psum(f"mlp_ps{k}", [P, 512]) for k in range(2)]

        ids_loaded = [sem(f"ids_loaded{u}") for u in range(BUFFERS)]
        rows_loaded = [sem(f"rows_loaded{c}") for c in range(chunks)]
        weights_loaded = sem("weights_loaded")
        ctx_loaded = sem("ctx_loaded")
        ident_filled = sem("ident_filled")
        ident_ready = sem("ident_ready")
        transposed = [sem(f"transposed{h}") for h in range(D_HALVES)]
        emb_copied = [sem(f"emb_copied{h}") for h in range(D_HALVES)]
        gram_done = [sem(f"gram_done{k}") for k in range(2)]
        dots_copied = [sem(f"dots_copied{k}") for k in range(2)]
        mlp_done = [sem(f"mlp_done{k}") for k in range(2)]
        mlp_copied = [sem(f"mlp_copied{k}") for k in range(2)]
        y_stored = sem("y_stored")
        pool_let_go = sem("pool_let_go")
        pe_let_go = sem("pe_let_go")

        def wait(eng, s, value):
            if not (isinstance(value, int) and value <= 0):
                eng.wait_ge(s, value)

        block = ctx.enter_context(nc.Block())

        @block.sync
        def _(sp):
            def load_ids(t, u):
                sp.dma_start(ids_sb[:, u, :], ids[bass.ds(t * P, P), :]).then_inc(ids_loaded[u], DMA)

            def reload_ids(t, u):
                sp.wait_ge(transposed[1], (t - BUFFERS + 1) * chunks * quads)
                load_ids(t, u)

            def load_ctx(t):
                if not isinstance(t, int) or t > 0:
                    sp.wait_ge(mlp_done[1], (t - 1) * FILLS[1] + PACK)
                sp.dma_start(packed[:, :, pairs_of_fields:],
                             dense_ctx[bass.ds(t * P, P), :].rearrange("(g s) c -> g s c", s=QUAD)
                             ).then_inc(ctx_loaded, DMA)

            def store_y(p):
                sp.wait_ge(mlp_copied[0], (p + 1) * BUFFERS * FILLS[0])
                sp.dma_start(y[bass.ds(p * BUFFERS * P, BUFFERS * P), :].rearrange("n o -> o n"), y_row[:]
                             ).then_inc(y_stored, DMA)

            load_ids(0, 0)
            load_ids(1, 1)
            sp.dma_start(w1_sb[:], w1.rearrange("(k p) n -> p k n", p=P)).then_inc(weights_loaded, DMA)
            sp.dma_start(w2_sb[:], w2.rearrange("(k p) n -> p k n", p=P)).then_inc(weights_loaded, DMA)
            with nc.allow_non_contiguous_dma(reason="columns of a few hundred words, once"):
                sp.dma_start(w3_sb[:], w3.rearrange("(k p) o -> p (k o)", p=P)).then_inc(weights_loaded, DMA)
                sp.dma_start(b1_sb[:], b1.rearrange("(k p) -> p k", p=P)).then_inc(weights_loaded, DMA)
                sp.dma_start(b2_sb[:], b2.rearrange("(k p) -> p k", p=P)).then_inc(weights_loaded, DMA)
            load_ctx(0)
            reload_ids(2, 0)
            load_ctx(1)
            with sp.Fori(1, tiles // BUFFERS - 1) as p:
                t = p * BUFFERS
                reload_ids(t + 1, 1)
                load_ctx(t)
                store_y(p - 1)
                reload_ids(t + 2, 0)
                load_ctx(t + 1)
            reload_ids(tiles - 1, 1)
            load_ctx(tiles - 2)
            store_y(tiles // BUFFERS - 2)
            load_ctx(tiles - 1)
            store_y(tiles // BUFFERS - 1)
            sp.wait_ge(y_stored, DMA * (tiles // BUFFERS))

        @block.gpsimd
        def _(pool):
            def gather_chunk(p, u, c):
                t = p * BUFFERS + u
                if c == 0:
                    pool.wait_ge(ids_loaded[u], (p + 1) * DMA)
                wait(pool, transposed[1], ((t - 1) * chunks + c + 1) * quads
                     if not isinstance(t, int) or t > 0 else 0)
                pool.sem_inc(pool_let_go, 1)
                for j in range(CHUNK):
                    f = c * CHUNK + j
                    pool.indirect_dma_start(
                        out=rows[c][:, j, :], out_offset=None, in_=tables[f],
                        in_offset=bass.IndirectOffsetOnAxis(ap=ids_sb[:, u, f:f + 1].bitcast(u32), axis=0),
                    ).then_inc(rows_loaded[c], DMA)

            gather_chunk(0, 0, 0)
            nc.gpsimd.memset(ident[:], 1.0).then_inc(ident_filled, 1)
            pool.wait_ge(ident_filled, 1)
            nc.gpsimd.affine_select(out=ident[:], in_=ident[:], compare_op=ALU.is_equal, fill=0.0, base=0,
                                    pattern=[[-1, P]], channel_multiplier=1).then_inc(ident_ready, 1)
            for c in range(1, chunks):
                gather_chunk(0, 0, c)
            for c in range(chunks):
                gather_chunk(0, 1, c)
            with pool.Fori(1, tiles // BUFFERS) as p:
                for u in range(BUFFERS):
                    for c in range(chunks):
                        gather_chunk(p, u, c)

        @block.tensor
        def _(pe):
            def transpose_quad(t, u, c, q):
                if q == 0:
                    pe.wait_ge(rows_loaded[c], (t + 1) * CHUNK * DMA)
                for h in range(D_HALVES):
                    wait(pe, emb_copied[h], (t * chunks + c) * quads + q - quads + 1)
                    for j in range(QUAD):
                        last = nc.tensor.transpose(tr_ps[h][q][:, j, :], rows[c][:, q * QUAD + j, h * P:(h + 1) * P],
                                                   ident[:])
                    last.then_inc(transposed[h], 1)

            def gram(t, u, part):
                for fill in (2 * part, 2 * part + 1):
                    if fill == 0:
                        for h in range(D_HALVES):
                            pe.wait_ge(emb_copied[h], (t + 1) * chunks * quads)
                    wait(pe, dots_copied[fill % 2], t * gram_fills_each + part)
                    for g in range(bank_groups):
                        s = (fill * bank_groups + g) * QUAD
                        for h in range(D_HALVES):
                            four = emb_t[u][:, h, s:s + QUAD, :].rearrange("p s f -> p (s f)")
                            last = nc.tensor.matmul(gram_ps[fill % 2][:, g, :], four, four,
                                                    start=(h == 0), stop=(h == D_HALVES - 1))
                    last.then_inc(gram_done[fill % 2], 1)

            def all_copied(t, fills):
                for k in range(2):
                    wait(pe, mlp_copied[k], t * FILLS[k] + min(fills, FILLS[k]))

            def tri(t):
                for k in range(2):
                    pe.wait_ge(dots_copied[k], (t + 1) * gram_fills_each)
                all_copied(t, 0)
                for k in range(2):
                    for i in range(k * per_transpose, fields, 2 * per_transpose):
                        at = tri_place(i)[2]
                        last = nc.tensor.transpose(mlp_ps[k][:, at:at + P], dots[:, i:i + per_transpose, :],
                                                   ident[:])
                    last.then_inc(mlp_done[k], 1)

            def pack(t):
                all_copied(t, TRI)
                pe.wait_ge(ctx_loaded, (t + 1) * DMA)
                pe.sem_inc(pe_let_go, 1)
                for k in range(2):
                    for j in range(k1 // 2):
                        for s in range(QUAD):
                            f = (k * k1 // 2 + j) * P
                            at = j * P + s * groups
                            last = nc.tensor.transpose(mlp_ps[k][:, at:at + groups], packed[:, s, f:f + P],
                                                       ident[0:groups, 0:groups])
                    last.then_inc(mlp_done[k], 1)

            def layer1(t):
                all_copied(t, PACK)
                for m in range(m1):
                    k = m * 2 // m1
                    at = (m % (m1 // 2)) * P
                    for i in range(k1):
                        last = nc.tensor.matmul(mlp_ps[k][:, at:at + P], w1_sb[:, i, m * P:(m + 1) * P],
                                                feat_t[:, i, :], start=(i == 0), stop=(i == k1 - 1))
                    if m % (m1 // 2) == m1 // 2 - 1:
                        last.then_inc(mlp_done[k], 1)

            def layer2(t):
                all_copied(t, LAYER1)
                for m in range(m2):
                    for i in range(m1):
                        last = nc.tensor.matmul(mlp_ps[m][:, 0:P], w2_sb[:, i, m * P:(m + 1) * P],
                                                hid1_t[:, i, :], start=(i == 0), stop=(i == m1 - 1))
                    last.then_inc(mlp_done[m], 1)

            def layer3(t):
                all_copied(t, LAYER2)
                for i in range(m2):
                    last = nc.tensor.matmul(mlp_ps[0][0:1, 0:P], w3_sb[:, i:i + 1], hid2_t[:, i, :],
                                            start=(i == 0), stop=(i == m2 - 1))
                last.then_inc(mlp_done[0], 1)

            def step(t, u):
                o = 1 - u
                gram(t - 1, o, 0)
                gram(t - 1, o, 1)
                transpose_quad(t, u, 0, 0)
                transpose_quad(t, u, 0, 1)
                gram(t - 1, o, 2)
                gram(t - 1, o, 3)
                transpose_quad(t, u, 1, 0)
                tri(t - 1)
                transpose_quad(t, u, 1, 1)
                pack(t - 1)
                layer1(t - 1)
                transpose_quad(t, u, 2, 0)
                layer2(t - 1)
                transpose_quad(t, u, 2, 1)
                transpose_quad(t, u, 3, 0)
                transpose_quad(t, u, 3, 1)
                layer3(t - 1)

            pe.wait_ge(ident_ready, 1)
            for c in range(chunks):
                for q in range(quads):
                    transpose_quad(0, 0, c, q)
            pe.wait_ge(weights_loaded, 5 * DMA)
            step(1, 1)
            with pe.Fori(1, tiles // BUFFERS) as p:
                for u in range(BUFFERS):
                    step(p * BUFFERS + u, u)
            for c in range(chunks):
                gram(tiles - 1, 1, c)
            for stage in (tri, pack, layer1, layer2, layer3):
                stage(tiles - 1)

        def copies(eng, who, copy, bias_relu):
            def emb_copy(t, u, c, q):
                f = c * CHUNK + q * QUAD
                eng.wait_ge(transposed[who], (t * chunks + c) * quads + q + 1)
                copy(emb_t[u][:, who, :, f:f + QUAD].rearrange("p s f -> p f s"), tr_ps[who][q][:]
                     ).then_inc(emb_copied[who], 1)

            def dots_copy(t, part):
                fill = 2 * part + who
                eng.wait_ge(gram_done[who], t * gram_fills_each + part + 1)
                for s in range(QUAD):
                    own = slice(s * fields, (s + 1) * fields)
                    of_fill = dots[own, :, fill * bank_groups:(fill + 1) * bank_groups]
                    last = copy(of_fill.rearrange("p f g -> p g f"), gram_ps[who][own, :, own])
                last.then_inc(dots_copied[who], 1)

            def stage_done(t, fills):
                eng.wait_ge(mlp_done[who], t * FILLS[who] + fills)

            def tri_copy(t):
                stage_done(t, TRI)
                for i in range(fields - 1):
                    bank, part, at = tri_place(i)
                    if bank == who:
                        n, to = fields - 1 - i, first_of_row(i)
                        seen = mlp_ps[who][part:part + groups, at:at + P].rearrange("g (s f) -> g s f", s=QUAD)
                        last = copy(packed[:, :, to:to + n], seen[:, :, i + 1:fields])
                last.then_inc(mlp_copied[who], 1)

            def pack_copy(t):
                stage_done(t, PACK)
                for j in range(k1 // 2):
                    last = copy(feat_t[:, who * k1 // 2 + j, :].rearrange("p (g s) -> p s g", s=QUAD),
                                mlp_ps[who][:, j * P:(j + 1) * P].rearrange("p (s g) -> p s g", s=QUAD))
                last.then_inc(mlp_copied[who], 1)

            def layer1_copy(t):
                stage_done(t, LAYER1)
                for j in range(m1 // 2):
                    m = who * m1 // 2 + j
                    last = bias_relu(hid1_t[:, m, :], mlp_ps[who][:, j * P:(j + 1) * P], b1_sb[:, m:m + 1])
                last.then_inc(mlp_copied[who], 1)

            def layer2_copy(t):
                stage_done(t, LAYER2)
                bias_relu(hid2_t[:, who, :], mlp_ps[who][:, 0:P], b2_sb[:, who:who + 1]).then_inc(mlp_copied[who], 1)

            def layer3_copy(t, u):
                if who == 0:
                    stage_done(t, LAYER3)
                    if u == 0:
                        wait(eng, y_stored, t // BUFFERS * DMA)
                    copy(y_row[:, u * P:(u + 1) * P], mlp_ps[0][0:1, 0:P]).then_inc(mlp_copied[0], 1)

            def step(t, u):
                o = 1 - u
                dots_copy(t - 1, 0)
                dots_copy(t - 1, 1)
                emb_copy(t, u, 0, 0)
                emb_copy(t, u, 0, 1)
                dots_copy(t - 1, 2)
                dots_copy(t - 1, 3)
                emb_copy(t, u, 1, 0)
                tri_copy(t - 1)
                emb_copy(t, u, 1, 1)
                pack_copy(t - 1)
                layer1_copy(t - 1)
                emb_copy(t, u, 2, 0)
                layer2_copy(t - 1)
                emb_copy(t, u, 2, 1)
                emb_copy(t, u, 3, 0)
                emb_copy(t, u, 3, 1)
                layer3_copy(t - 1, o)

            for c in range(chunks):
                for q in range(quads):
                    emb_copy(0, 0, c, q)
            eng.wait_ge(weights_loaded, 5 * DMA)
            step(1, 1)
            with eng.Fori(1, tiles // BUFFERS) as p:
                for u in range(BUFFERS):
                    step(p * BUFFERS + u, u)
            for c in range(4):
                dots_copy(tiles - 1, c)
            for stage in (tri_copy, pack_copy, layer1_copy, layer2_copy):
                stage(tiles - 1)
            layer3_copy(tiles - 1, 1)

        @block.vector
        def _(dve):
            copies(dve, 0, nc.vector.tensor_copy,
                   lambda out, x, bias: nc.vector.tensor_scalar(out, x, bias, 0.0, ALU.add, ALU.max))

        @block.scalar
        def _(act):
            copies(act, 1, nc.scalar.copy,
                   lambda out, x, bias: nc.scalar.activation(out, x, ACT.Relu, bias=bias))


def kernel(**inputs):
    import numpy as np
    import concourse.bacc as bacc
    from concourse.bass_utils import run_bass_kernel_spmd

    nc = bacc.Bacc("TRN2", target_bir_lowering=False, num_devices=1)
    arrays, aps = {}, {}
    for name, a in inputs.items():
        a = np.ascontiguousarray(a)
        arrays[f"in_{name}"] = a
        aps[name] = nc.dram_tensor(f"in_{name}", a.shape, mybir.dt.from_np(a.dtype), kind="ExternalInput").ap()
    batch, fields = inputs["ids"].shape
    y = nc.dram_tensor("out_y", (batch, 1), mybir.dt.float32, kind="ExternalOutput").ap()
    build(nc, aps["dense_ctx"], aps["ids"], [aps[f"tbl_{f}"] for f in range(fields)],
          aps["W_top1"], aps["b_top1"], aps["W_top2"], aps["b_top2"], aps["W_top3"], y)
    r = run_bass_kernel_spmd(nc, [arrays], core_ids=[0])
    return r.results[0]["out_y"]
```

```python
import concourse.bass as bass
from concourse import mybir
from contextlib import ExitStack

P = 128
D_HALVES = 2
QUAD = 4
CHUNK = 8
BUFFERS = 2
DMA = 16
SELECTED = (27, 31)
SELECT_CHUNKS = 8


def squares(fields):
    first, side = 0, fields // 2
    while side:
        yield first, side
        first += fields // 2 * side
        side //= 2


def rows_of_w1(fields, features):
    rows = []
    for _, side in squares(fields):
        for b in range(fields // 2 // side):
            for i in range(2 * b * side, (2 * b + 1) * side):
                for j in range((2 * b + 1) * side, (2 * b + 2) * side):
                    rows.append(i * (fields - 1) - i * (i - 1) // 2 + j - i - 1)
    return rows + list(range(len(rows), features))


def build(nc, dense_ctx, ids, ids_by_field, table_row_numbers, tables, w1, b1, w2, b2, w3, y):
    f32, i32, u32, f32r = mybir.dt.float32, mybir.dt.int32, mybir.dt.uint32, mybir.dt.float32r
    ALU, ACT = mybir.AluOpType, mybir.ActivationFunctionType

    batch, fields = ids.shape
    width = tables[0].shape[1]
    ctx_width = dense_ctx.shape[1]
    h1, h2 = w1.shape[1], w2.shape[1]
    pairs_of_fields = fields * (fields - 1) // 2
    features = pairs_of_fields + ctx_width
    tiles = batch // P
    chunks = fields // CHUNK
    quads = CHUNK // QUAD
    groups = P // QUAD
    firsts = fields - 1
    bank_groups = 4
    gram_fills = groups // bank_groups
    gram_fills_each = gram_fills // 2
    k1, m1, m2 = features // P, h1 // P, h2 // P
    assert width == D_HALVES * P and features == k1 * P and fields == groups == P // QUAD
    assert chunks == 4 and m1 == 4 and m2 == 2 and tiles % BUFFERS == 0

    pair_cols = BUFFERS * P
    select_rows = tables[SELECTED[0]].shape[0] // SELECT_CHUNKS
    assert all(tables[f].shape[0] == SELECT_CHUNKS * select_rows for f in SELECTED) and select_rows <= P

    def gathered(c, q):
        return [f for f in range(c * CHUNK + q * QUAD, c * CHUNK + (q + 1) * QUAD) if f not in SELECTED]

    TURN, LAYER1, LAYER2, LAYER3 = 1, 2, 3, 4
    FILLS = (LAYER3, LAYER2)

    with ExitStack() as ctx:
        def sbuf(name, shape, dt=f32):
            return ctx.enter_context(nc.sbuf_tensor(name, shape, dt))

        def psum(name, shape):
            return ctx.enter_context(nc.psum_tensor(name, shape, f32))

        def sem(name):
            return ctx.enter_context(nc.semaphore(name))

        ids_sb = sbuf("ids_sb", [P, BUFFERS, fields], i32)
        rows = [sbuf(f"rows{c}", [P, CHUNK, width]) for c in range(chunks)]
        emb_t = [sbuf(f"emb_t{u}", [P, D_HALVES, P, fields]) for u in range(BUFFERS)]
        dots = sbuf("dots", [P, firsts, groups])
        dots_t = sbuf("dots_t", [P, (fields + 1) * fields])
        packed = sbuf("packed", [P, features])
        feat_t = sbuf("feat_t", [P, k1, P])
        hid1_t = sbuf("hid1_t", [P, m1, P])
        hid2_t = sbuf("hid2_t", [P, m2, P])
        y_sb = sbuf("y_sb", [P, BUFFERS])
        w1_sb = sbuf("w1_sb", [P, k1, h1])
        w2_sb = sbuf("w2_sb", [P, m1, h2])
        w3_sb = sbuf("w3_sb", [P, m2])
        b1_sb = sbuf("b1_sb", [P, m1])
        b2_sb = sbuf("b2_sb", [P, m2])
        ident = sbuf("ident", [P, P])
        n_sel = len(SELECTED)
        sel_raw = emb_t[1][0:select_rows].rearrange("p h s f -> p (h s f)")[
            :, 0:n_sel * SELECT_CHUNKS * width].rearrange("p (n c w) -> p n c w", n=n_sel, c=SELECT_CHUNKS)
        sel_high = sbuf("sel_high", [select_rows, n_sel, SELECT_CHUNKS, width], f32r)
        sel_low = sbuf("sel_low", [select_rows, n_sel, SELECT_CHUNKS, width], f32r)
        sel_ids = sbuf("sel_ids", [select_rows, n_sel, pair_cols], i32)
        onehot = sbuf("onehot", [select_rows, n_sel, SELECT_CHUNKS, pair_cols], f32r)
        row_numbers = sbuf("row_numbers", [select_rows, SELECT_CHUNKS])

        tr_ps = [[psum(f"tr_ps{h}{q}", [P, QUAD, P]) for q in range(quads)] for h in range(D_HALVES)]
        gram_ps = [psum(f"gram_ps{k}", [P, bank_groups * P]) for k in range(2)]
        gram_out = [gram_ps[k][:, 0:bank_groups * QUAD * firsts].rearrange("p (g n) -> p g n", g=bank_groups)
                    for k in range(2)]
        mlp_ps = gram_ps
        sel_ps = [psum(f"sel_ps{n}", [P, D_HALVES, pair_cols]) for n in range(n_sel)]

        ids_loaded = [sem(f"ids_loaded{u}") for u in range(BUFFERS)]
        rows_loaded = [[sem(f"rows_loaded{c}{q}") for q in range(quads)] for c in range(chunks)]
        tables_loaded = sem("tables_loaded")
        tables_high = sem("tables_high")
        tables_split = sem("tables_split")
        sel_ids_loaded = sem("sel_ids_loaded")
        onehot_built = sem("onehot_built")
        selected = sem("selected")
        selected_copied = sem("selected_copied")
        weights_loaded = sem("weights_loaded")
        ctx_loaded = sem("ctx_loaded")
        ident_filled = sem("ident_filled")
        ident_ready = sem("ident_ready")
        transposed = [sem(f"transposed{h}") for h in range(D_HALVES)]
        emb_copied = [sem(f"emb_copied{h}") for h in range(D_HALVES)]
        dots_spread = sem("dots_spread")
        packed_ready = [sem(f"packed_ready{k}") for k in range(2)]
        gram_done = [sem(f"gram_done{k}") for k in range(2)]
        dots_copied = [sem(f"dots_copied{k}") for k in range(2)]
        mlp_done = [sem(f"mlp_done{k}") for k in range(2)]
        mlp_copied = [sem(f"mlp_copied{k}") for k in range(2)]
        y_stored = sem("y_stored")
        pool_let_go = sem("pool_let_go")

        def wait(eng, s, value):
            if not (isinstance(value, int) and value <= 0):
                eng.wait_ge(s, value)

        block = ctx.enter_context(nc.Block())

        @block.sync
        def _(sp):
            def load_ids(t, u):
                sp.dma_start(ids_sb[:, u, :], ids[bass.ds(t * P, P), :]).then_inc(ids_loaded[u], DMA)

            def reload_ids(t, u):
                sp.wait_ge(transposed[1], (t - BUFFERS + 1) * chunks * quads)
                load_ids(t, u)

            def load_ctx(t):
                if not isinstance(t, int) or t > 0:
                    sp.wait_ge(mlp_done[1], (t - 1) * FILLS[1] + TURN)
                sp.dma_start(packed[:, pairs_of_fields:], dense_ctx[bass.ds(t * P, P), :]).then_inc(ctx_loaded, DMA)

            def store_y(p):
                sp.wait_ge(mlp_copied[0], (p + 1) * BUFFERS * FILLS[0])
                with nc.allow_non_contiguous_dma(reason="the results, a word per sample"):
                    sp.dma_start(y[bass.ds(p * BUFFERS * P, BUFFERS * P), :].rearrange("(u p) o -> p (u o)", p=P),
                                 y_sb[:]).then_inc(y_stored, DMA)

            def load_sel_ids(p):
                wait(sp, onehot_built, p)
                for n, f in enumerate(SELECTED):
                    sp.dma_start(sel_ids[:, n, :], ids_by_field[f:f + 1, bass.ds(p * pair_cols, pair_cols)]
                                 .to_broadcast([select_rows, pair_cols])).then_inc(sel_ids_loaded, DMA)

            load_ids(0, 0)
            load_sel_ids(0)
            for n, f in enumerate(SELECTED):
                sp.dma_start(sel_raw[:, n], tables[f].rearrange("(c p) w -> p c w", p=select_rows)
                             ).then_inc(tables_loaded, DMA)
            sp.dma_start(row_numbers[:], table_row_numbers).then_inc(tables_loaded, DMA)
            load_ids(1, 1)
            sp.dma_start(w1_sb[:], w1.rearrange("(k p) n -> p k n", p=P)).then_inc(weights_loaded, DMA)
            sp.dma_start(w2_sb[:], w2.rearrange("(k p) n -> p k n", p=P)).then_inc(weights_loaded, DMA)
            with nc.allow_non_contiguous_dma(reason="columns of a few hundred words, once"):
                sp.dma_start(w3_sb[:], w3.rearrange("(k p) o -> p (k o)", p=P)).then_inc(weights_loaded, DMA)
                sp.dma_start(b1_sb[:], b1.rearrange("(k p) -> p k", p=P)).then_inc(weights_loaded, DMA)
                sp.dma_start(b2_sb[:], b2.rearrange("(k p) -> p k", p=P)).then_inc(weights_loaded, DMA)
            load_ctx(0)
            load_sel_ids(1)
            reload_ids(2, 0)
            load_ctx(1)
            with sp.Fori(1, tiles // BUFFERS - 1) as p:
                t = p * BUFFERS
                reload_ids(t + 1, 1)
                load_sel_ids(p + 1)
                load_ctx(t)
                store_y(p - 1)
                reload_ids(t + 2, 0)
                load_ctx(t + 1)
            reload_ids(tiles - 1, 1)
            load_ctx(tiles - 2)
            store_y(tiles // BUFFERS - 2)
            load_ctx(tiles - 1)
            store_y(tiles // BUFFERS - 1)
            sp.wait_ge(y_stored, DMA * (tiles // BUFFERS))

        @block.gpsimd
        def _(pool):
            def gather_chunk(p, u, c):
                t = p * BUFFERS + u
                if c == 0:
                    pool.wait_ge(ids_loaded[u], (p + 1) * DMA)
                wait(pool, transposed[1], ((t - 1) * chunks + c + 1) * quads
                     if not isinstance(t, int) or t > 0 else 0)
                pool.sem_inc(pool_let_go, 1)
                for q in range(quads):
                    for f in gathered(c, q):
                        pool.indirect_dma_start(
                            out=rows[c][:, f - c * CHUNK, :], out_offset=None, in_=tables[f],
                            in_offset=bass.IndirectOffsetOnAxis(ap=ids_sb[:, u, f:f + 1].bitcast(u32), axis=0),
                        ).then_inc(rows_loaded[c][q], DMA)

            gather_chunk(0, 0, 0)
            nc.gpsimd.memset(ident[:], 1.0).then_inc(ident_filled, 1)
            pool.wait_ge(ident_filled, 1)
            nc.gpsimd.affine_select(out=ident[:], in_=ident[:], compare_op=ALU.is_equal, fill=0.0, base=0,
                                    pattern=[[-1, P]], channel_multiplier=1).then_inc(ident_ready, 1)
            for c in range(1, chunks):
                gather_chunk(0, 0, c)
            for c in range(chunks):
                gather_chunk(0, 1, c)
            with pool.Fori(1, tiles // BUFFERS) as p:
                for u in range(BUFFERS):
                    for c in range(chunks):
                        gather_chunk(p, u, c)

        @block.tensor
        def _(pe):
            def transpose_quad(t, u, c, q):
                pe.wait_ge(rows_loaded[c][q], (t + 1) * len(gathered(c, q)) * DMA)
                for h in range(D_HALVES):
                    wait(pe, emb_copied[h], (t * chunks + c) * quads + q - quads + 1)
                    for f in gathered(c, q):
                        j = f - c * CHUNK
                        last = nc.tensor.transpose(tr_ps[h][q][:, j - q * QUAD, :], rows[c][:, j, h * P:(h + 1) * P],
                                                   ident[:])
                    last.then_inc(transposed[h], 1)

            def gram(t, u, part):
                for fill in (2 * part, 2 * part + 1):
                    if fill == 0:
                        for h in range(D_HALVES):
                            pe.wait_ge(emb_copied[h], (t + 1) * chunks * quads)
                        if u == 0:
                            pe.wait_ge(selected_copied, t // BUFFERS + 1)
                    if part == 0:
                        wait(pe, mlp_copied[fill % 2], t * FILLS[fill % 2])
                    else:
                        wait(pe, dots_copied[fill % 2], t * gram_fills_each + part)
                    for g in range(bank_groups):
                        s = (fill * bank_groups + g) * QUAD
                        for h in range(D_HALVES):
                            four = emb_t[u][:, h, s:s + QUAD, :]
                            last = nc.tensor.matmul(gram_out[fill % 2][:, g, :], four.rearrange("p s f -> p (s f)"),
                                                    four[:, :, 0:firsts],
                                                    start=(h == 0), stop=(h == D_HALVES - 1))
                    last.then_inc(gram_done[fill % 2], 1)

            def all_copied(t, fills):
                for k in range(2):
                    wait(pe, mlp_copied[k], t * FILLS[k] + min(fills, FILLS[k]))

            def turn(t):
                all_copied(t, 0)
                for k in range(2):
                    pe.wait_ge(packed_ready[k], t + 1)
                pe.wait_ge(ctx_loaded, (t + 1) * DMA)
                for i in range(k1):
                    k, j = i * 2 // k1, i % (k1 // 2)
                    last = nc.tensor.transpose(mlp_ps[k][:, j * P:(j + 1) * P], packed[:, i * P:(i + 1) * P],
                                               ident[:])
                    if j == k1 // 2 - 1:
                        last.then_inc(mlp_done[k], 1)

            def layer1(t):
                all_copied(t, TURN)
                for m in range(m1):
                    k = m * 2 // m1
                    at = (m % (m1 // 2)) * P
                    for i in range(k1):
                        last = nc.tensor.matmul(mlp_ps[k][:, at:at + P], w1_sb[:, i, m * P:(m + 1) * P],
                                                feat_t[:, i, :], start=(i == 0), stop=(i == k1 - 1))
                    if m % (m1 // 2) == m1 // 2 - 1:
                        last.then_inc(mlp_done[k], 1)

            def layer2(t):
                all_copied(t, LAYER1)
                for m in range(m2):
                    for i in range(m1):
                        last = nc.tensor.matmul(mlp_ps[m][:, 0:P], w2_sb[:, i, m * P:(m + 1) * P],
                                                hid1_t[:, i, :], start=(i == 0), stop=(i == m1 - 1))
                    last.then_inc(mlp_done[m], 1)

            def layer3(t):
                all_copied(t, LAYER2)
                for i in range(m2):
                    last = nc.tensor.matmul(mlp_ps[0][:, 0:1], hid2_t[:, i, :], w3_sb[:, i:i + 1],
                                            start=(i == 0), stop=(i == m2 - 1))
                last.then_inc(mlp_done[0], 1)

            def select(p, h, part):
                if p is None:
                    return
                if h == 0 and part == 0:
                    pe.wait_ge(onehot_built, p + 1)
                    wait(pe, selected_copied, p)
                for n in range(n_sel):
                    for c in range(part * SELECT_CHUNKS // 4, (part + 1) * SELECT_CHUNKS // 4):
                        for table in (sel_high, sel_low):
                            last = nc.tensor.matmul(sel_ps[n][:, h, :], table[:, n, c, h * P:(h + 1) * P],
                                                    onehot[:, n, c, :], start=(c == 0 and table is sel_high),
                                                    stop=(c == SELECT_CHUNKS - 1 and table is sel_low))
                if h == D_HALVES - 1 and part == 3:
                    last.then_inc(selected, 1)

            def step(t, u, pair):
                o = 1 - u
                h = o
                gram(t - 1, o, 0)
                gram(t - 1, o, 1)
                transpose_quad(t, u, 0, 0)
                transpose_quad(t, u, 0, 1)
                gram(t - 1, o, 2)
                gram(t - 1, o, 3)
                transpose_quad(t, u, 1, 0)
                transpose_quad(t, u, 1, 1)
                select(pair, h, 0)
                select(pair, h, 1)
                turn(t - 1)
                if u == 0:
                    select(pair, h, 2)
                    select(pair, h, 3)
                    layer1(t - 1)
                    transpose_quad(t, u, 2, 0)
                else:
                    transpose_quad(t, u, 2, 0)
                    layer1(t - 1)
                    select(pair, h, 2)
                if pair is None:
                    transpose_quad(t, u, 2, 1)
                    transpose_quad(t, u, 3, 0)
                    layer2(t - 1)
                    transpose_quad(t, u, 3, 1)
                    layer3(t - 1)
                else:
                    layer2(t - 1)
                    transpose_quad(t, u, 2, 1)
                    transpose_quad(t, u, 3, 0)
                    layer3(t - 1)
                    transpose_quad(t, u, 3, 1)
                if u == 1:
                    select(pair, h, 3)

            pe.wait_ge(ident_ready, 1)
            for c in range(chunks):
                for q in range(quads):
                    transpose_quad(0, 0, c, q)
                if c == 1:
                    pe.wait_ge(tables_split, 1)
                if c > 1:
                    for part in range(4):
                        select(0, c - 2, part)
            pe.wait_ge(weights_loaded, 5 * DMA)
            step(1, 1, 1)
            with pe.Fori(1, tiles // BUFFERS - 1) as p:
                step(p * BUFFERS, 0, p)
                step(p * BUFFERS + 1, 1, p + 1)
            step(tiles - 2, 0, tiles // BUFFERS - 1)
            step(tiles - 1, 1, None)
            for c in range(chunks):
                gram(tiles - 1, 1, c)
            for stage in (turn, layer1, layer2, layer3):
                stage(tiles - 1)

        def copies(eng, who, copy, bias_relu):
            def emb_copy(t, u, c, q):
                fs = gathered(c, q)
                j, n = fs[0] % QUAD, len(fs)
                eng.wait_ge(transposed[who], (t * chunks + c) * quads + q + 1)
                copy(emb_t[u][:, who, :, fs[0]:fs[0] + n].rearrange("p (g s) f -> p f s g", s=QUAD),
                     tr_ps[who][q][:, j:j + n, :].rearrange("p f (s g) -> p f s g", s=QUAD)
                     ).then_inc(emb_copied[who], 1)

            def dots_copy(t, part):
                fill = 2 * part + who
                eng.wait_ge(gram_done[who], t * gram_fills_each + part + 1)
                for s in range(QUAD):
                    own = slice(s * fields, (s + 1) * fields)
                    of_fill = dots[own, :, fill * bank_groups:(fill + 1) * bank_groups]
                    last = copy(of_fill.rearrange("p f g -> p g f"),
                                gram_out[who][own, :, s * firsts:(s + 1) * firsts])
                last.then_inc(dots_copied[who], 1)

            def stage_done(t, fills):
                eng.wait_ge(mlp_done[who], t * FILLS[who] + fills)

            def spread(t):
                if who == 0:
                    for k in range(2):
                        eng.wait_ge(dots_copied[k], (t + 1) * gram_fills_each)
                    nc.vector.transpose(dots_t[:, 0:firsts * fields], dots[:].rearrange("p f g -> p (f g)")
                                        ).then_inc(dots_spread, 1)

            def pack_copy(t):
                eng.wait_ge(dots_spread, t + 1)
                for first, side in squares(fields):
                    if (side == fields // 2) == (who == 1):
                        count = fields // 2 // side
                        seen = dots_t[:].rearrange("p (b x) -> p b x", b=count)[:, :, 0:side * fields]
                        seen = seen.rearrange("p b (i j) -> p b i j", j=fields)[:, :, :, side:2 * side]
                        to = packed[:, first:first + count * side * side]
                        last = copy(to.rearrange("p (b i j) -> p b i j", b=count, j=side), seen)
                last.then_inc(packed_ready[who], 1)

            def turn_copy(t):
                stage_done(t, TURN)
                half = slice(who * k1 // 2, (who + 1) * k1 // 2)
                copy(feat_t[:, half, :], mlp_ps[who][:, 0:k1 // 2 * P].rearrange("p (k s) -> p k s", s=P)
                     ).then_inc(mlp_copied[who], 1)

            def layer1_copy(t):
                stage_done(t, LAYER1)
                for j in range(m1 // 2):
                    m = who * m1 // 2 + j
                    last = bias_relu(hid1_t[:, m, :], mlp_ps[who][:, j * P:(j + 1) * P], b1_sb[:, m:m + 1])
                last.then_inc(mlp_copied[who], 1)

            def layer2_copy(t):
                stage_done(t, LAYER2)
                bias_relu(hid2_t[:, who, :], mlp_ps[who][:, 0:P], b2_sb[:, who:who + 1]).then_inc(mlp_copied[who], 1)

            def layer3_copy(t, u):
                if who == 0:
                    stage_done(t, LAYER3)
                    if u == 0:
                        wait(eng, y_stored, t // BUFFERS * DMA)
                    copy(y_sb[:, u:u + 1], mlp_ps[0][:, 0:1]).then_inc(mlp_copied[0], 1)

            def selection(p):
                if who == 1:
                    eng.wait_ge(selected, p + 1)
                    for n, f in enumerate(SELECTED):
                        for u in range(BUFFERS):
                            last = copy(emb_t[u][:, :, :, f].rearrange("p h (g s) -> p h s g", s=QUAD),
                                        sel_ps[n][:, :, u * P:(u + 1) * P].rearrange("p h (s g) -> p h s g", s=QUAD))
                    last.then_inc(selected_copied, 1)
                elif not (isinstance(p, int) and p == tiles // BUFFERS - 1):
                    build_onehot(p + 1)

            def build_onehot(p):
                eng.wait_ge(sel_ids_loaded, (p + 1) * n_sel * DMA)
                wait(eng, selected, p)
                for n in range(n_sel):
                    for c in range(SELECT_CHUNKS):
                        last = nc.vector.tensor_scalar(onehot[:, n, c, :], sel_ids[:, n, :],
                                                       row_numbers[:, c:c + 1], None, ALU.is_equal)
                last.then_inc(onehot_built, 1)

            def step(t, u, pair):
                o = 1 - u
                dots_copy(t - 1, 0)
                dots_copy(t - 1, 1)
                emb_copy(t, u, 0, 0)
                emb_copy(t, u, 0, 1)
                dots_copy(t - 1, 2)
                dots_copy(t - 1, 3)
                spread(t - 1)
                if who == 0:
                    pack_copy(t - 1)
                emb_copy(t, u, 1, 0)
                if who == 1:
                    pack_copy(t - 1)
                emb_copy(t, u, 1, 1)
                turn_copy(t - 1)
                if u == 0:
                    selection(pair)
                if u == 0:
                    layer1_copy(t - 1)
                emb_copy(t, u, 2, 0)
                if u == 1:
                    layer1_copy(t - 1)
                if pair is None:
                    emb_copy(t, u, 2, 1)
                    emb_copy(t, u, 3, 0)
                    layer2_copy(t - 1)
                    emb_copy(t, u, 3, 1)
                    layer3_copy(t - 1, o)
                else:
                    layer2_copy(t - 1)
                    emb_copy(t, u, 2, 1)
                    emb_copy(t, u, 3, 0)
                    layer3_copy(t - 1, o)
                    emb_copy(t, u, 3, 1)

            if who == 0:
                eng.wait_ge(tables_loaded, (n_sel + 1) * DMA)
                copy(sel_high[:], sel_raw).then_inc(tables_high, 1)
                eng.wait_ge(tables_high, 1)
                nc.vector.tensor_tensor(sel_low[:], sel_raw, sel_high[:].bitcast(f32), ALU.subtract
                                        ).then_inc(tables_split, 1)
                build_onehot(0)
            for c in range(chunks):
                for q in range(quads):
                    emb_copy(0, 0, c, q)
            if who == 1:
                eng.wait_ge(tables_split, 1)
            selection(0)
            eng.wait_ge(weights_loaded, 5 * DMA)
            step(1, 1, 1)
            with eng.Fori(1, tiles // BUFFERS - 1) as p:
                step(p * BUFFERS, 0, p)
                step(p * BUFFERS + 1, 1, p + 1)
            step(tiles - 2, 0, tiles // BUFFERS - 1)
            step(tiles - 1, 1, None)
            for c in range(4):
                dots_copy(tiles - 1, c)
            for stage in (spread, pack_copy, turn_copy, layer1_copy, layer2_copy):
                stage(tiles - 1)
            layer3_copy(tiles - 1, 1)

        @block.vector
        def _(dve):
            copies(dve, 0, nc.vector.tensor_copy,
                   lambda out, x, bias: nc.vector.tensor_scalar(out, x, bias, 0.0, ALU.add, ALU.max))

        @block.scalar
        def _(act):
            copies(act, 1, nc.scalar.copy,
                   lambda out, x, bias: nc.scalar.activation(out, x, ACT.Relu, bias=bias))


def kernel(**inputs):
    import numpy as np
    import concourse.bacc as bacc
    from concourse.bass_utils import run_bass_kernel_spmd

    nc = bacc.Bacc("TRN2", target_bir_lowering=False, num_devices=1)
    arrays, aps = {}, {}
    for name, a in list(inputs.items()):
        a = np.ascontiguousarray(a)
        inputs[name] = a
    inputs["ids_by_field"] = np.ascontiguousarray(inputs["ids"].T)
    rows = inputs[f"tbl_{SELECTED[0]}"].shape[0] // SELECT_CHUNKS
    numbers = np.arange(rows * SELECT_CHUNKS, dtype=np.float32)
    inputs["table_row_numbers"] = numbers.reshape(SELECT_CHUNKS, rows).T.copy()
    inputs["W_top1"] = inputs["W_top1"][rows_of_w1(inputs["ids"].shape[1], inputs["W_top1"].shape[0])]
    for name, a in inputs.items():
        arrays[f"in_{name}"] = a
        aps[name] = nc.dram_tensor(f"in_{name}", a.shape, mybir.dt.from_np(a.dtype), kind="ExternalInput").ap()
    batch, fields = inputs["ids"].shape
    y = nc.dram_tensor("out_y", (batch, 1), mybir.dt.float32, kind="ExternalOutput").ap()
    build(nc, aps["dense_ctx"], aps["ids"], aps["ids_by_field"], aps["table_row_numbers"],
          [aps[f"tbl_{f}"] for f in range(fields)],
          aps["W_top1"], aps["b_top1"], aps["W_top2"], aps["b_top2"], aps["W_top3"], y)
    r = run_bass_kernel_spmd(nc, [arrays], core_ids=[0])
    return r.results[0]["out_y"]
```
